# Optimizing a Trainium2 kernel written in Bass

```python
import numpy as np
import jax
import jax.numpy as jnp

def _softmax(x, axis=-1):
    return jax.nn.softmax(x, axis=axis)

def _gelu(x):
    return jax.nn.gelu(x, approximate=True)

def _silu(x):
    return jax.nn.silu(x)

def _sigmoid(x):
    return jax.nn.sigmoid(x)

def _layernorm(x, axis=-1, eps=1e-05):
    m = jnp.mean(x, axis=axis, keepdims=True)
    v = jnp.var(x, axis=axis, keepdims=True)
    return (x - m) / jnp.sqrt(v + eps)

def _scatter_add(tgt, idx, src, axis=0):
    return tgt.at[idx].add(src)

def _segment_sum(src, seg, n):
    return jax.ops.segment_sum(src, seg, n)
kernel_name = 'mk_adj_resnorm_d2_adj_r2_fdd50c'

def setup_inputs(seed: int=0):
    np.random.seed(seed)
    _w = jnp.asarray

    def _rec_inputs():
        import jax
        import jax.numpy as jnp
        _gk = jax.random.key(seed)
        x = -0.000929 + 1 * jax.random.normal(jax.random.fold_in(_gk, 1), (8192, 64), jnp.float32)
        _a = jax.random.bernoulli(jax.random.fold_in(_gk, 2), 0.000244141, (8192, 8192))
        _a = jnp.logical_or(_a, jnp.swapaxes(_a, -1, -2))
        _a = jnp.logical_or(_a, jnp.eye(8192, dtype=bool))
        _af = _a.astype(jnp.float32)
        _af = _af * jax.random.uniform(jax.random.fold_in(_gk, 3), (8192, 8192), jnp.float32, 0.05, 1)
        adj = _af
        return (x, adj)
    x, adj = _rec_inputs()

    def _L0_gnn_setup():
        import jax, jax.numpy as jnp
        import numpy as np
        P_DROP = 0.1
        key = jax.random.key(seed)
        k1, k2, k3 = jax.random.split(key, 3)
        N, D = (8192, 64)
        x = jax.random.normal(k1, (N, D), dtype=jnp.float32)
        adj = jax.random.uniform(k2, (N, N), dtype=jnp.float32)
        u = jax.random.uniform(k3, (N, D), dtype=jnp.float32)
        return {'x': x, 'adj': adj, 'u': u}
    _L0_gnn_all = _L0_gnn_setup()
    _L0_gnn_in = {k: v for k, v in _L0_gnn_all.items() if k in ('u',)}
    del _L0_gnn_all

    def _L1_gnn_setup():
        import jax, jax.numpy as jnp
        import numpy as np
        N = 8192
        IN_F = 64
        OUT_F = 64
        key = jax.random.key(seed)
        k_x, k_adj, k_w = jax.random.split(key, 3)
        x = jax.random.normal(k_x, (N, IN_F), dtype=jnp.float32)
        adj = jax.random.uniform(k_adj, (N, N), dtype=jnp.float32)
        std = float(np.sqrt(2.0 / (IN_F + OUT_F)))
        weight = jax.random.normal(k_w, (IN_F, OUT_F), dtype=jnp.float32) * std
        bias = jnp.zeros((OUT_F,), dtype=jnp.float32)
        return {'x': x, 'adj': adj, 'weight': weight, 'bias': bias}
    _L1_gnn_all = _L1_gnn_setup()
    _L1_gnn_in = {k: v for k, v in _L1_gnn_all.items() if k in ('weight', 'bias')}
    del _L1_gnn_all
    return {'x': x, 'adj': adj, 'L0_gnn_u': _L0_gnn_in['u'], 'L1_gnn_weight': _L1_gnn_in['weight'], 'L1_gnn_bias': _L1_gnn_in['bias']}

def reference(x, adj, L0_gnn_u, L1_gnn_weight, L1_gnn_bias):
    import jax
    import jax.numpy as jnp

    def _L0_gnn_ref(x, adj, u):
        import jax, jax.numpy as jnp
        import numpy as np
        P_DROP = 0.1
        keep = (u >= P_DROP).astype(x.dtype)
        x_drop = x * keep / (1.0 - P_DROP)
        return jnp.matmul(adj, x_drop)

    def _L1_gnn_ref(x, adj, weight, bias):
        import jax, jax.numpy as jnp
        import numpy as np
        N = 8192
        IN_F = 64
        OUT_F = 64
        support = jnp.matmul(x, weight)
        output = jnp.matmul(adj, support)
        return output + bias
    x = _layernorm(x + _L0_gnn_ref(x, adj, L0_gnn_u), axis=-1)
    x = _layernorm(x + _L1_gnn_ref(x, adj, L1_gnn_weight, L1_gnn_bias), axis=-1)
    return x

_drawn_inputs = setup_inputs


def setup_inputs(seed=0):
    import zlib

    import numpy as np

    out = dict(_drawn_inputs(seed))
    spreads = {'L1_gnn_bias': (0.0, 0.1)}
    factors = {}
    for name, (base, spread) in spreads.items():
        noise = np.random.default_rng([zlib.crc32(name.encode()), seed]).standard_normal(out[name].shape)
        drawn = base * np.exp(spread * noise) if base else spread * noise
        out[name] = jnp.asarray(drawn.astype(out[name].dtype))
    for name, factor in factors.items():
        out[name] = (out[name] * factor).astype(out[name].dtype)
    return out
```

```python
import concourse.bass as bass
from concourse import mybir
from contextlib import ExitStack

F32 = mybir.dt.float32
ALU = mybir.AluOpType
ACT = mybir.ActivationFunctionType
AX = mybir.AxisListType

P = 128
N = 8192
D = 64
C = 4
B = C * P
NB = N // B
DROP = 0.1
EPS = 1e-5

SLOTS = 17
HOLD = 3
HOLD_MORE = (1, 3, 5, 7, 9)
FILL = 2
ECHO_BANKS = 3
XU_GROUP = 4


def held(i, j):
    return i <= j <= i + HOLD + (i in HOLD_MORE) or (i, j) == (1, 0)


def merge(a, b):
    n, m = len(a), len(b)
    keyed = [((k + 0.5) / n, 0, x) for k, x in enumerate(a)] + [((k + 0.5) / m, 1, x) for k, x in enumerate(b)]
    return [x for _, _, x in sorted(keyed, key=lambda t: t[:2])]


def order_of_work():
    jobs = []
    again = []
    for i in range(NB):
        ready = [("fused", i, j) for j in range(i - 1) if i >= 2]
        late = [("fused", i, i - 1)] if i >= 2 else [("first", i, j) for j in range(i)]
        far = [("first", i, j) for j in range(i + 1, NB) if not held(i, j)]
        near = [("first", i, j) for j in range(NB - 1, i - 1, -1) if held(i, j)]
        if i == 1:
            ready, late = late, []
        if i >= 1:
            filler = []
            for _ in range(FILL):
                filler.append((ready or far).pop(0))
            jobs.append(filler[0])
            jobs.append(("turn", i - 1))
            jobs += filler[1:]
            jobs += [("second", r, i - 1) for r in range(NB) if held(r, i - 1)]
            again += [("second", r, i - 1) for r in range(i - 1) if not held(r, i - 1)]
        quota = max(0, min(len(again) - (3 if i == NB - 1 else 0), round((1.61 * i - 8.6) / 1.1)))
        now, again = again[:quota], again[quota:]
        rest = merge(ready + late, far)
        jobs += merge(rest, now)
        jobs += near
        jobs.append(("row_end", i))
    jobs += again[:2]
    jobs.append(("turn", NB - 1))
    jobs += again[2:]
    last = [("second", r, NB - 1) for r in range(NB) if held(r, NB - 1)]
    last += [("second", r, NB - 1) for r in range(NB) if not held(r, NB - 1)]
    for n, job in enumerate(last):
        jobs.append(job)
        if n >= 1:
            jobs.append(("final", last[n - 1][1]))
    jobs.append(("final", last[-1][1]))
    return jobs


TILE_JOBS = ("fused", "first", "second")


def place_tiles(jobs):
    tile_jobs = [job for job in jobs if job[0] in TILE_JOBS]
    needs, on_chip = [], {}
    for m, (kind, i, j) in enumerate(tile_jobs):
        if (i, j) not in on_chip:
            on_chip[i, j] = len(needs)
            needs.append([i, j, m, m])
        needs[on_chip[i, j]][3] = m
        if not (kind == "first" and held(i, j)):
            del on_chip[i, j]
    free = [(0, s, 0) for s in range(SLOTS)]
    loads, slot_of = [], {}
    for i, j, begin, end in needs:
        free.sort()
        freed, slot, use = free.pop(0)
        assert freed <= begin, "the order of work needs more slots"
        loads.append((i, j, slot, use, freed))
        free.append((end + 1, slot, use + 1))
        slot_of[begin] = slot_of[end] = (slot, use)
    return loads, slot_of


def resnorm_graph_layers(nc, x, adj_t, u, weight, bias, out):
    jobs = order_of_work()
    loads, slot_of = place_tiles(jobs)

    done_after, n_tile_jobs = {}, 0
    for job in jobs:
        if job[0] in TILE_JOBS:
            n_tile_jobs += 1
        done_after[job] = n_tile_jobs
    seconds = [job for job in jobs if job[0] == "second"]
    finals = [job[1] for job in jobs if job[0] == "final"]
    complete = {i: max(n for n, job in enumerate(seconds) if job[1] == i) + 1 for i in range(NB)}

    x_v = x.rearrange("(b p c) d -> p b (c d)", p=P, c=C)
    u_v = u.rearrange("(b p c) d -> p b (c d)", p=P, c=C)
    out_v = out.rearrange("(b p c) d -> b p (c d)", p=P, c=C)

    ctx = ExitStack()
    with ctx:
        def sb(name, shape):
            return ctx.enter_context(nc.sbuf_tensor(name, shape, F32))

        def sem(name):
            return ctx.enter_context(nc.semaphore(name))

        tiles = sb("tiles", [P, SLOTS, C, B])
        stat = sb("stat", [P, NB * C, 2 * D])
        layer2 = sb("layer2", [P, NB, B])
        x_res = sb("x_res", [P, 2, C * D])
        halves = sb("halves", [P, B])
        r = sb("r", [P, C, D])
        sq = sb("sq", [P, C, D])
        sums = sb("sums", [P, C])
        vsum = sb("vsum", [P, C])
        var = sb("var", [P, C])
        root = sb("root", [P, C])
        newton = sb("newton", [P, C])
        rstd = sb("rstd", [P, C])
        h_bias = x_res[:, :, :].rearrange("p n (c d) -> p n c d", c=C)
        y = halves[:, :].rearrange("p (n c d) -> p n c d", n=2, c=C)
        w2 = sb("w2", [P, 2 * D])
        ident = sb("ident", [P, P])
        bias_b = sb("bias_b", [P, D])

        half = SLOTS - 4
        x_stage = tiles[:, half:half + 2].rearrange("p s c b -> p (s c b)").rearrange("p (b k) -> p b k", k=C * D)
        u_stage = tiles[:, half + 2:half + 4].rearrange("p s c b -> p (s c b)").rearrange("p (b k) -> p b k", k=C * D)

        banks = [ctx.enter_context(nc.psum_tensor(f"bank{n}", [P, B], F32)) for n in range(8)]
        sum_a = banks[0:2]
        sum_b = banks[2:4]
        turned = banks[4]
        echo = banks[5:8]
        product = [banks[4], banks[(NB - 2) % 2]]

        s_arrived = [sem(f"tile_arrived_{n}") for n in range(SLOTS)]
        s_xu = [sem(f"xu_loaded_{n}") for n in range(NB // XU_GROUP)]
        s_res = [sem(f"x_res_loaded_{n}") for n in range(2)]
        s_small = sem("weight_bias_loaded")
        s_out = [sem(f"out_stored_{n}") for n in range(2)]
        tile_jobs_done = sem("tile_jobs_done")
        dropped = sem("x_dropped")
        zeroed = sem("layer2_zeroed")
        identity = sem("identity_ready")
        evac_a = sem("sum_a_left_psum")
        evac_b = sem("sum_b_left_psum")
        turned_ready = sem("block_turned")
        turned_read = sem("turned_read")
        squared = sem("squared")
        centred = sem("centred")
        var_ready = sem("variance_ready")
        rooted = sem("root_ready")
        h_ready = sem("h_ready")
        added = sem("second_added")
        product_ready = sem("product_ready")
        product_read = sem("product_read")
        hb_ready = sem("h_bias_ready")
        y_ready = sem("y_ready")
        pool_step = sem("pool_step")
        dve_step = sem("dve_step")

        order_xu = []
        for kind, i, j in [job for job in jobs if job[0] in TILE_JOBS][:NB]:
            if j // XU_GROUP not in order_xu:
                order_xu.append(j // XU_GROUP)

        block = ctx.enter_context(nc.Block())

        @block.sync
        def _(sp):
            def load_xu(g):
                b = slice(g * XU_GROUP, (g + 1) * XU_GROUP)
                sp.dma_start(u_stage[:, b], u_v[:, b]).then_inc(s_xu[g], 16)
                sp.dma_start(x_stage[:, b], x_v[:, b]).then_inc(s_xu[g], 16)

            load_xu(order_xu[0])
            rows_begun = 0
            for n, (i, j, slot, use, freed) in enumerate(loads):
                if n in (1, 3, 5):
                    load_xu(order_xu[(n + 1) // 2])
                if n == 7:
                    for at in (0, D):
                        for beside in (0, D):
                            sp.dma_start(w2[at:at + D, beside:beside + D], weight).then_inc(s_small, 16)
                    sp.dma_start(bias_b[:, :], bias.rearrange("(a d) -> a d", a=1).to_broadcast([P, D])).then_inc(s_small, 16)
                if i == rows_begun:
                    if i >= 2:
                        sp.wait_ge(turned_read, i - 1)
                    sp.dma_start(x_res[:, i % 2], x_v[:, i]).then_inc(s_res[i % 2], 16)
                    rows_begun += 1
                if use == 0 and slot >= half:
                    sp.wait_ge(dropped, NB // XU_GROUP)
                if freed:
                    sp.wait_ge(tile_jobs_done, freed)
                sp.dma_start(tiles[:, slot], adj_t[i, j]).then_inc(s_arrived[slot], 16)
            for n, i in enumerate(finals):
                sp.wait_ge(y_ready, n + 1)
                sp.dma_start(out_v[i], y[:, n % 2].rearrange("p c d -> p (c d)")).then_inc(s_out[n % 2], 16)
            for stored in s_out:
                sp.wait_ge(stored, 16 * NB // 2)

        @block.gpsimd
        def _(pool):
            pool.memset(layer2[:, :, :], 0.0).then_inc(zeroed, 1)
            pool.memset(ident[:, :], 0.0).then_inc(pool_step, 1)
            pool.wait_ge(pool_step, 1)
            pool.affine_select(out=ident[:, :], in_=ident[:, :], compare_op=ALU.not_equal, fill=1.0,
                               base=0, pattern=[[-1, P]], channel_multiplier=1).then_inc(identity, 1)
            pool.wait_ge(s_small, 5 * 16)
            pool.wait_ge(turned_read, NB)
            for n, i in enumerate(finals):
                if n >= 2:
                    pool.wait_ge(product_read, n - 1)
                pool.wait_ge(h_ready, i + 1)
                pool.tensor_tensor(out=h_bias[:, n % 2], in0=stat[:, i * C:(i + 1) * C, D:2 * D],
                                   in1=bias_b[:, :].unsqueeze(1).to_broadcast([P, C, D]),
                                   op=ALU.add).then_inc(hb_ready, 1)

        @block.scalar
        def _(act):
            norms = 0

            def norm():
                nonlocal norms
                act.wait_ge(centred, norms + 1)
                act.activation(sq[:, :, :], r[:, :, :], ACT.Square).then_inc(squared, 1)
                norms += 1
                act.wait_ge(var_ready, norms)
                act.activation(root[:, :], var[:, :], ACT.Sqrt).then_inc(rooted, 1)

            for job in jobs:
                if job[0] == "row_end":
                    i = job[1]
                    if i == 0:
                        act.wait_ge(zeroed, 1)
                    else:
                        act.wait_ge(turned_ready, i)
                    act.wait_ge(tile_jobs_done, done_after[job])
                    act.activation(halves[0:D, :], sum_a[i % 2][0:D, :], ACT.Copy).then_inc(evac_a, 1)
                    if i >= 2:
                        act.activation(layer2[D:P, i], sum_a[i % 2][D:P, :], ACT.Copy).then_inc(evac_a, 1)
                elif job[0] in ("turn", "final"):
                    norm()

        @block.vector
        def _(dve):
            steps = 0
            norms = 0
            n_second = 0
            n_final = 0

            def step(instruction):
                nonlocal steps
                steps += 1
                instruction.then_inc(dve_step, 1)
                dve.wait_ge(dve_step, steps)

            def over_features(v):
                return v[:, :].unsqueeze(2).to_broadcast([P, C, D])

            def normalise(result):
                nonlocal norms
                step(dve.tensor_reduce(out=sums[:, :], in_=r[:, :, :], axis=AX.X, op=ALU.add))
                dve.scalar_tensor_tensor(out=r[:, :, :], in0=over_features(sums), scalar=-1.0 / D,
                                         in1=r[:, :, :], op0=ALU.mult, op1=ALU.add).then_inc(centred, 1)
                norms += 1
                dve.wait_ge(squared, norms)
                step(dve.tensor_reduce(out=vsum[:, :], in_=sq[:, :, :], axis=AX.X, op=ALU.add))
                dve.tensor_scalar(var[:, :], vsum[:, :], 1.0 / D, EPS, ALU.mult, ALU.add).then_inc(var_ready, 1)
                dve.wait_ge(rooted, norms)
                step(dve.reciprocal(rstd[:, :], root[:, :]))
                step(dve.tensor_tensor(out=newton[:, :], in0=rstd[:, :], in1=rstd[:, :], op=ALU.mult))
                step(dve.scalar_tensor_tensor(out=newton[:, :], in0=newton[:, :], scalar=-0.5, in1=var[:, :],
                                              op0=ALU.mult, op1=ALU.mult))
                step(dve.scalar_tensor_tensor(out=rstd[:, :], in0=newton[:, :], scalar=1.5, in1=rstd[:, :],
                                              op0=ALU.add, op1=ALU.mult))
                return dve.tensor_tensor(out=result, in0=r[:, :, :], in1=over_features(rstd), op=ALU.mult)

            for n, g in enumerate(order_xu):
                dve.wait_ge(s_xu[g], 32)
                t = slice(g * XU_GROUP * C, (g + 1) * XU_GROUP * C)
                b = slice(g * XU_GROUP, (g + 1) * XU_GROUP)
                step(dve.scalar_tensor_tensor(
                    out=stat[:, t, 0:D], in0=u_stage[:, b].rearrange("p b (c d) -> p (b c) d", d=D), scalar=DROP,
                    in1=x_stage[:, b].rearrange("p b (c d) -> p (b c) d", d=D), op0=ALU.is_ge, op1=ALU.mult))
                dve.tensor_scalar(stat[:, t, 0:D], stat[:, t, 0:D], 1.0 / (1.0 - DROP), None, ALU.mult).then_inc(dropped, 1)

            for job in jobs:
                if job[0] == "second":
                    i = job[1]
                    if n_second == 0:
                        dve.wait_ge(zeroed, 1)
                    if n_second and i >= 2:
                        dve.wait_ge(evac_a, 2 * (i + 1) - 2)
                    if n_second:
                        dve.wait_ge(added, n_second)
                    dve.wait_ge(tile_jobs_done, done_after[job])
                    dve.tensor_tensor(out=layer2[:, i], in0=echo[n_second % ECHO_BANKS][:, :], in1=layer2[:, i],
                                      op=ALU.add).then_inc(added, 1)
                    n_second += 1
                elif job[0] == "row_end":
                    i = job[1]
                    if i >= 1:
                        dve.wait_ge(turned_ready, i)
                    dve.wait_ge(tile_jobs_done, done_after[job])
                    dve.tensor_copy(halves[D:P, :], sum_b[i % 2][D:P, :]).then_inc(evac_b, 1)
                elif job[0] == "turn":
                    i = job[1]
                    t = turned[:, :].rearrange("p (c f) -> p c f", c=C)
                    dve.wait_ge(s_res[i % 2], 16 * (i // 2 + 1))
                    if i:
                        dve.wait_ge(h_ready, i)
                    dve.wait_ge(turned_ready, i + 1)
                    step(dve.tensor_tensor(out=r[:, :, :], in0=t[:, :, 0:D],
                                           in1=x_res[:, i % 2].rearrange("p (c d) -> p c d", c=C), op=ALU.add))
                    dve.tensor_tensor(out=r[:, :, :], in0=t[:, :, D:2 * D], in1=r[:, :, :],
                                      op=ALU.add).then_inc(turned_read, 1)
                    dve.wait_ge(turned_read, i + 1)
                    normalise(stat[:, i * C:(i + 1) * C, D:2 * D]).then_inc(h_ready, 1)
                elif job[0] == "final":
                    t = product[n_final % 2][:, :].rearrange("p (c f) -> p c f", c=C)
                    dve.wait_ge(hb_ready, n_final + 1)
                    dve.wait_ge(product_ready, n_final + 1)
                    if n_final == 0:
                        dve.wait_ge(h_ready, NB)
                    else:
                        dve.wait_ge(y_ready, n_final)
                    dve.tensor_tensor(out=r[:, :, :], in0=t[:, :, 0:D], in1=h_bias[:, n_final % 2],
                                      op=ALU.add).then_inc(product_read, 1)
                    dve.wait_ge(product_read, n_final + 1)
                    if n_final >= 2:
                        dve.wait_ge(s_out[n_final % 2], 16 * (n_final // 2))
                    normalise(y[:, n_final % 2]).then_inc(y_ready, 1)
                    n_final += 1

        @block.tensor
        def _(pe):
            m = 0
            n_second = 0
            n_final = 0
            first_of_row = True
            xu_seen = 0
            h_seen = 0
            first_alone = {}
            for job in jobs:
                if job[0] == "first":
                    first_alone.setdefault(job[1], job)

            def arrived(m):
                slot, use = slot_of[m]
                pe.wait_ge(s_arrived[slot], 16 * (use + 1))
                return tiles[:, slot]

            for at, job in enumerate(jobs):
                kind = job[0]
                if kind in ("fused", "first"):
                    _, i, j = job
                    tile = arrived(m)
                    if i == 0:
                        k = order_xu.index(j // XU_GROUP) + 1
                        if k > xu_seen:
                            pe.wait_ge(dropped, k)
                            xu_seen = k
                    if first_of_row and i >= 2:
                        pe.wait_ge(evac_a, max(i - 1, 2 * (i - 1) - 2))
                        pe.wait_ge(evac_b, i - 1)
                    ends = jobs[at + 1] == ("row_end", i)
                    for c in range(C):
                        if kind == "fused":
                            last = pe.matmul(sum_a[i % 2][:, :], stat[:, j * C + c, :], tile[:, c],
                                             start=first_of_row and c == 0, stop=False, skip_group_check=True)
                        elif c % 2 == 0:
                            last = pe.matmul(sum_a[i % 2][0:D, :], stat[:, j * C + c, 0:D], tile[:, c],
                                             start=first_of_row and i < 2 and c == 0, stop=ends and c == 2,
                                             skip_group_check=True)
                        else:
                            last = pe.matmul(sum_b[i % 2][D:P, :], stat[:, j * C + c, 0:D], tile[:, c],
                                             start=("first", i, j) == first_alone[i] and c == 1, stop=ends and c == 3,
                                             skip_group_check=True)
                    last.then_inc(tile_jobs_done, 1)
                    m += 1
                    first_of_row = False
                elif kind == "second":
                    _, i, j = job
                    tile = arrived(m)
                    if j + 1 > h_seen:
                        pe.wait_ge(h_ready, j + 1)
                        h_seen = j + 1
                    if n_second >= ECHO_BANKS:
                        pe.wait_ge(added, n_second - ECHO_BANKS + 1)
                    bank = echo[n_second % ECHO_BANKS]
                    for c in range(C):
                        to = slice(0, D) if c % 2 == 0 else slice(D, P)
                        last = pe.matmul(bank[to, :], stat[:, j * C + c, D:2 * D], tile[:, c],
                                         start=c < 2, stop=c >= 2)
                    last.then_inc(tile_jobs_done, 1)
                    m += 1
                    n_second += 1
                elif kind == "row_end":
                    first_of_row = True
                elif kind == "turn":
                    i = job[1]
                    if i == 0:
                        pe.wait_ge(identity, 1)
                    else:
                        pe.wait_ge(turned_read, i)
                    pe.wait_ge(evac_a, max(i + 1, 2 * (i + 1) - 2 - (i >= 2)))
                    pe.wait_ge(evac_b, i + 1)
                    for c in range(C):
                        last = pe.transpose(turned[:, c * P:(c + 1) * P], halves[:, c * P:(c + 1) * P], ident[:, :])
                    last.then_inc(turned_ready, 1)
                elif kind == "final":
                    i = job[1]
                    if n_final == 0:
                        pe.wait_ge(s_small, 5 * 16)
                        pe.wait_ge(turned_read, NB)
                        pe.wait_ge(evac_a, 2 * NB - 2)
                    else:
                        if n_final >= 2:
                            pe.wait_ge(product_read, n_final - 1)
                    pe.wait_ge(added, complete[i])
                    for c in range(C):
                        last = pe.matmul(product[n_final % 2][:, c * P:(c + 1) * P], layer2[:, i, c * P:(c + 1) * P],
                                         w2[:, :], start=True, stop=True)
                    last.then_inc(product_ready, 1)
                    n_final += 1


_OUT = ((N, D), "float32")


def kernel(x, adj, L0_gnn_u, L1_gnn_weight, L1_gnn_bias):
    import numpy as np
    import concourse.bacc as bacc
    from concourse.bass_utils import run_bass_kernel_spmd

    a = np.asarray(adj).reshape(NB, P, C, NB, P, C).transpose(0, 3, 4, 5, 2, 1)
    arrays = {
        "x": np.ascontiguousarray(x),
        "adj_t": np.ascontiguousarray(a).reshape(NB, NB, P, C, B),
        "u": np.ascontiguousarray(L0_gnn_u),
        "weight": np.ascontiguousarray(L1_gnn_weight),
        "bias": np.ascontiguousarray(L1_gnn_bias),
    }
    nc = bacc.Bacc("TRN2", target_bir_lowering=False, num_devices=1)
    args = [nc.dram_tensor(name, v.shape, F32, kind="ExternalInput").ap() for name, v in arrays.items()]
    out = nc.dram_tensor("out", _OUT[0], F32, kind="ExternalOutput").ap()
    resnorm_graph_layers(nc, *args, out)
    r = run_bass_kernel_spmd(nc, [arrays], core_ids=[0])
    return r.results[0]["out"]
```

```python
import concourse.bass as bass
from concourse import mybir
from contextlib import ExitStack

F32 = mybir.dt.float32
ALU = mybir.AluOpType
ACT = mybir.ActivationFunctionType
AX = mybir.AxisListType

P = 128
N = 8192
D = 64
C = 4
B = C * P
NB = N // B
DROP = 0.1
EPS = 1e-5

SLOTS = 17
LENT = (3, 2, 1)
HOLD = (4, 5, 4, 4, 3, 4, 5, 3, 3, 5, 4, 3, 7, 2, 3, 3)
AGAIN = (0, 0, 0, 0, 0, 16, 3, 13, 13, 5, 10, 1, 8, 0, 3, 0)
FILL = 4
ECHO_BANKS = 3
RUN = 3
XU_GROUPS = ((5, 6), (6, 9), (9, 12), (12, 16), (0, 5))


XU_BEFORE = (1, 3, 6, 9)


def held(i, j):
    return i <= j <= i + HOLD[i] or (i, j) == (1, 0)


def merge(a, b):
    n, m = len(a), len(b)
    keyed = [((k + 0.5) / n, 0, x) for k, x in enumerate(a)] + [((k + 0.5) / m, 1, x) for k, x in enumerate(b)]
    return [x for _, _, x in sorted(keyed, key=lambda t: t[:2])]


def in_runs(a, n):
    return [a[k:k + n] for k in range(0, len(a), n)]


def order_of_work():
    jobs = []
    again = []
    for i in range(NB):
        ready = [("fused", i, j) for j in range(i - 1) if i >= 2]
        late = [("fused", i, i - 1)] if i >= 2 else [("first", i, j) for j in range(i)]
        far = [("first", i, j) for j in range(i + 1, NB) if not held(i, j)]
        near = [("first", i, j) for j in range(NB - 1, i - 1, -1) if held(i, j)]
        if i == 1:
            ready, late = late, []
        if i >= 1:
            filler = []
            for _ in range(FILL):
                filler.append((ready or far).pop(0))
            jobs.append(filler[0])
            jobs.append(("turn", i - 1))
            jobs += filler[1:]
            jobs += [("second", r, i - 1) for r in range(NB) if held(r, i - 1)]
            again += [("second", r, i - 1) for r in range(i - 1) if not held(r, i - 1)]
        quota = min(len(again), AGAIN[i])
        now, again = again[:quota], again[quota:]
        jobs += [job for run in merge(in_runs(ready + late, RUN), in_runs(merge(far, now), RUN)) for job in run]
        jobs += near
        jobs.append(("row_end", i))
    jobs += again[:1]
    jobs.append(("turn", NB - 1))
    jobs += again[1:]
    pending = None
    for i in range(NB - 2, -1, -2):
        jobs.append(("second", i + 1, NB - 1))
        jobs.append(("second", i, NB - 1))
        if pending is not None:
            jobs.append(("final", pending))
        pending = i
    jobs.append(("final", pending))
    return jobs


TILE_JOBS = ("fused", "first", "second")


def place_tiles(jobs):
    tile_jobs = [job for job in jobs if job[0] in TILE_JOBS]
    needs, on_chip = [], {}
    for m, (kind, i, j) in enumerate(tile_jobs):
        if (i, j) not in on_chip:
            on_chip[i, j] = len(needs)
            needs.append([i, j, m, m])
        needs[on_chip[i, j]][3] = m
        if not (kind == "first" and held(i, j)):
            del on_chip[i, j]
    until = {}
    for s in range(SLOTS + len(LENT)):
        until[s] = len(tile_jobs)
        if s >= SLOTS:
            row_end = jobs.index(("row_end", LENT[s - SLOTS] * C - 1))
            until[s] = sum(job[0] in TILE_JOBS for job in jobs[:row_end])
    free = [(0, s, 0) for s in [*range(SLOTS - 4), *range(SLOTS, SLOTS + len(LENT)), *range(SLOTS - 4, SLOTS)]]
    loads, slot_of, given_back = [], {}, {}
    for i, j, begin, end in needs:
        free.sort(key=lambda t: t[0])
        found = next(t for t in free if end < until[t[1]])
        free.remove(found)
        freed, slot, use = found
        assert freed <= begin, "the order of work needs more slots"
        loads.append((i, j, slot, use, freed))
        free.append((end + 1, slot, use + 1))
        slot_of[begin] = slot_of[end] = (slot, use)
        given_back[slot] = end + 1
    return loads, slot_of, given_back


def resnorm_graph_layers(nc, x, adj_t, u, weight, bias, out):
    jobs = order_of_work()
    loads, slot_of, given_back = place_tiles(jobs)

    done_after, n_tile_jobs = {}, 0
    for job in jobs:
        if job[0] in TILE_JOBS:
            n_tile_jobs += 1
        done_after[job] = n_tile_jobs
    seconds = [job for job in jobs if job[0] == "second"]
    finals = [job[1] for job in jobs if job[0] == "final"]
    complete = {i: max(n for n, job in enumerate(seconds) if job[1] in (i, i + 1)) + 1 for i in range(0, NB, 2)}

    x_v = x.rearrange("(b p c) d -> p b (c d)", p=P, c=C)
    u_v = u.rearrange("(b p c) d -> p b (c d)", p=P, c=C)
    out_v = out.rearrange("(b p c) d -> p b (c d)", p=P, c=C)

    ctx = ExitStack()
    with ctx:
        def sb(name, shape):
            return ctx.enter_context(nc.sbuf_tensor(name, shape, F32))

        def sem(name):
            return ctx.enter_context(nc.semaphore(name))

        tiles = sb("tiles", [P, SLOTS, C, B])
        stat = sb("stat", [P, NB * C, 2 * D])
        layer2 = sb("layer2", [P, NB, B])
        x_res = sb("x_res", [P, 2, C * D])
        halves = sb("halves", [P, B])
        r = sb("r", [P, C, D])
        sq = sb("sq", [P, C, D])
        sums = sb("sums", [P, 2 * C])
        vsum = sb("vsum", [P, 2 * C])
        var = sb("var", [P, 2, 2 * C])
        root = sb("root", [P, 2, 2 * C])
        newton = sb("newton", [P, 2 * C])
        rstd = sb("rstd", [P, 2, 2 * C])
        h_bias = [x_res[:, :, :].rearrange("p n (c d) -> p (n c) d", d=D),
                  halves[:, :].rearrange("p (c d) -> p c d", d=D)]
        w2 = sb("w2", [P, 2 * D])
        ident = sb("ident", [P, P])
        bias_b = sb("bias_b", [P, D])

        half = SLOTS - 4
        def slot_ap(slot):
            if slot < SLOTS:
                return tiles[:, slot]
            return layer2[:, LENT[slot - SLOTS] * C:(LENT[slot - SLOTS] + 1) * C]

        x_stage = tiles[:, half:half + 2].rearrange("p s c b -> p (s c b)").rearrange("p (b k) -> p b k", k=C * D)
        u_stage = tiles[:, half + 2:half + 4].rearrange("p s c b -> p (s c b)").rearrange("p (b k) -> p b k", k=C * D)

        psum = ctx.enter_context(nc.psum_tensor("psum", [P, 8, B], F32))
        banks = [psum[:, n] for n in range(8)]
        sum_a = banks[0:2]
        sum_b = banks[2:4]
        turned = banks[4]
        echo = banks[5:8]
        product = [psum[:, 2 * n:2 * n + 2].rearrange("p b (c f) -> p (b c) f", c=C) for n in range(2)]

        def over_features(v):
            return v.unsqueeze(2).to_broadcast([*v.shape, D])

        def output_rows(n):
            return layer2[:, finals[n]].rearrange("p (c d) -> p c d", d=D)

        def output_squares(n):
            return layer2[:, finals[n] + 1].rearrange("p (c d) -> p c d", d=D)

        s_arrived = [sem(f"tile_arrived_{n}") for n in range(SLOTS + len(LENT))]
        s_xu = [sem(f"xu_loaded_{n}") for n in range(len(XU_GROUPS))]
        s_res = [sem(f"x_res_loaded_{n}") for n in range(2)]
        s_small = sem("weight_bias_loaded")
        s_out = sem("out_stored")
        tile_jobs_done = sem("tile_jobs_done")
        dropped = sem("x_dropped")
        zeroed = sem("layer2_zeroed")
        identity = sem("identity_ready")
        evac_a = sem("sum_a_left_psum")
        evac_b = sem("sum_b_left_psum")
        turned_ready = sem("block_turned")
        turned_read = sem("turned_read")
        squared = sem("squared")
        centred = sem("centred")
        var_ready = sem("variance_ready")
        rooted = sem("root_ready")
        rstd_ready = sem("output_scale_ready")
        h_ready = sem("h_ready")
        added = sem("second_added")
        product_ready = sem("product_ready")
        product_read = sem("product_read")
        hb_ready = sem("h_bias_ready")
        y_ready = sem("y_ready")
        pool_step = sem("pool_step")
        dve_step = sem("dve_step")

        row_0 = [job[2] for job in jobs if job[0] in TILE_JOBS][:NB]
        assert row_0 == sorted(row_0, key=lambda j: [a <= j < b for a, b in XU_GROUPS].index(True))

        block = ctx.enter_context(nc.Block())

        @block.sync
        def _(sp):
            def load_xu(g):
                b = slice(*XU_GROUPS[g])
                sp.dma_start(u_stage[:, b], u_v[:, b]).then_inc(s_xu[g], 16)
                sp.dma_start(x_stage[:, b], x_v[:, b]).then_inc(s_xu[g], 16)

            load_xu(0)
            rows_begun = 0
            for n, (i, j, slot, use, freed) in enumerate(loads):
                if n in XU_BEFORE:
                    load_xu(XU_BEFORE.index(n) + 1)
                if n == 7:
                    for at in (0, D):
                        for beside in (0, D):
                            sp.dma_start(w2[at:at + D, beside:beside + D], weight).then_inc(s_small, 16)
                    sp.dma_start(bias_b[:, :], bias.rearrange("(a d) -> a d", a=1).to_broadcast([P, D])).then_inc(s_small, 16)
                if i == rows_begun:
                    if i >= 2:
                        sp.wait_ge(turned_read, i - 1)
                    sp.dma_start(x_res[:, i % 2], x_v[:, i]).then_inc(s_res[i % 2], 16)
                    rows_begun += 1
                if use == 0 and half <= slot < SLOTS:
                    sp.wait_ge(dropped, len(XU_GROUPS))
                if freed:
                    sp.wait_ge(tile_jobs_done, freed)
                sp.dma_start(slot_ap(slot), adj_t[i, j]).then_inc(s_arrived[slot], 16)
            for n, i in enumerate(finals):
                sp.wait_ge(y_ready, n + 1)
                sp.dma_start(out_v[:, i:i + 2], layer2[:, i].rearrange("p (b k) -> p b k", b=2)).then_inc(s_out, 16)
            sp.wait_ge(s_out, 16 * len(finals))

        @block.gpsimd
        def _(pool):
            pool.memset(layer2[:, 0:C], 0.0).then_inc(zeroed, 1)
            pool.memset(ident[:, :], 0.0).then_inc(pool_step, 1)
            pool.wait_ge(pool_step, 1)
            pool.affine_select(out=ident[:, :], in_=ident[:, :], compare_op=ALU.not_equal, fill=1.0,
                               base=0, pattern=[[-1, P]], channel_multiplier=1).then_inc(identity, 1)
            for g in range(1, NB // C):
                if g in LENT:
                    pool.wait_ge(tile_jobs_done, given_back[SLOTS + LENT.index(g)])
                pool.memset(layer2[0:D, g * C:(g + 1) * C], 0.0).then_inc(zeroed, 1)
            pool.wait_ge(s_small, 5 * 16)
            pool.wait_ge(turned_read, NB)
            pool.wait_ge(turned_ready, NB)
            pool.wait_ge(h_ready, NB)

            def scale_pair(n):
                pool.wait_ge(rstd_ready, n + 1)
                pool.tensor_tensor(out=output_rows(n), in0=output_rows(n), in1=over_features(rstd[:, n % 2]),
                                   op=ALU.mult).then_inc(y_ready, 1)

            for n, i in enumerate(finals):
                if n >= 2:
                    pool.wait_ge(product_read, n - 1)
                pool.tensor_tensor(out=h_bias[n % 2], in0=stat[:, i * C:(i + 2) * C, D:2 * D],
                                   in1=bias_b[:, :].unsqueeze(1).to_broadcast([P, 2 * C, D]),
                                   op=ALU.add).then_inc(hb_ready, 1)
                if n >= 2:
                    scale_pair(n - 2)
            scale_pair(len(finals) - 2)

        @block.scalar
        def _(act):
            norms = 0

            def norm(squares, centred_rows, root_ap, var_ap):
                nonlocal norms
                norms += 1
                act.wait_ge(centred, norms)
                act.activation(squares, centred_rows, ACT.Square).then_inc(squared, 1)
                act.wait_ge(var_ready, norms)
                act.activation(root_ap, var_ap, ACT.Sqrt).then_inc(rooted, 1)

            for job in jobs:
                if job[0] == "row_end":
                    i = job[1]
                    if i:
                        act.wait_ge(turned_ready, i)
                    act.wait_ge(tile_jobs_done, done_after[job])
                    act.activation(halves[0:D, :], sum_a[i % 2][0:D, :], ACT.Copy).then_inc(evac_a, 1)
                    if i >= 2:
                        if i % C == 0:
                            act.wait_ge(zeroed, i // C + 1)
                        act.activation(layer2[D:P, i], sum_a[i % 2][D:P, :], ACT.Copy).then_inc(evac_a, 1)
                elif job[0] == "turn":
                    norm(sq[:, :, :], r[:, :, :], root[:, 0, 0:C], var[:, 0, 0:C])
                elif job[0] == "final":
                    i = job[1]
                    n = finals.index(i) % 2
                    norm(layer2[:, i + 1], layer2[:, i], root[:, n], var[:, n])

        @block.vector
        def _(dve):
            steps = 0
            norms = 0
            n_second = 0
            n_final = 0

            def step(instruction):
                nonlocal steps
                steps += 1
                instruction.then_inc(dve_step, 1)
                dve.wait_ge(dve_step, steps)

            def centre(rows, n):
                nonlocal norms
                step(dve.tensor_reduce(out=sums[:, 0:n], in_=rows, axis=AX.X, op=ALU.add))
                dve.scalar_tensor_tensor(out=rows, in0=over_features(sums[:, 0:n]),
                                         scalar=-1.0 / D, in1=rows, op0=ALU.mult, op1=ALU.add).then_inc(centred, 1)
                norms += 1

            def variance(squares, var_ap, n):
                dve.wait_ge(squared, norms)
                step(dve.tensor_reduce(out=vsum[:, 0:n], in_=squares, axis=AX.X, op=ALU.add))
                dve.tensor_scalar(var_ap, vsum[:, 0:n], 1.0 / D, EPS, ALU.mult, ALU.add).then_inc(var_ready, 1)

            def inverse_root(rstd_ap, var_ap, root_ap, n, norm):
                dve.wait_ge(rooted, norm)
                step(dve.reciprocal(rstd_ap, root_ap))
                step(dve.tensor_tensor(out=newton[:, 0:n], in0=rstd_ap, in1=rstd_ap, op=ALU.mult))
                step(dve.scalar_tensor_tensor(out=newton[:, 0:n], in0=newton[:, 0:n], scalar=-0.5, in1=var_ap,
                                              op0=ALU.mult, op1=ALU.mult))
                return dve.scalar_tensor_tensor(out=rstd_ap, in0=newton[:, 0:n], scalar=1.5, in1=rstd_ap,
                                                op0=ALU.add, op1=ALU.mult)

            def pair_inverse_root(n):
                if n >= 2:
                    dve.wait_ge(y_ready, n - 1)
                return inverse_root(rstd[:, n % 2], var[:, n % 2], root[:, n % 2], 2 * C, NB + n + 1)

            for n, (begin, end) in enumerate(XU_GROUPS):
                dve.wait_ge(s_xu[n], 32)
                b = slice(begin, end)
                t = slice(begin * C, end * C)
                step(dve.scalar_tensor_tensor(
                    out=stat[:, t, 0:D], in0=u_stage[:, b].rearrange("p b (c d) -> p (b c) d", d=D), scalar=DROP,
                    in1=x_stage[:, b].rearrange("p b (c d) -> p (b c) d", d=D), op0=ALU.is_ge, op1=ALU.mult))
                dve.tensor_scalar(stat[:, t, 0:D], stat[:, t, 0:D], 1.0 / (1.0 - DROP), None, ALU.mult).then_inc(dropped, 1)

            for job in jobs:
                if job[0] == "second":
                    i = job[1]
                    if n_second == 0:
                        dve.wait_ge(zeroed, 1)
                    if n_second and i >= 2:
                        dve.wait_ge(evac_a, 2 * (i + 1) - 2)
                    if n_second:
                        dve.wait_ge(added, n_second)
                    dve.wait_ge(tile_jobs_done, done_after[job])
                    dve.tensor_tensor(out=layer2[:, i], in0=echo[n_second % ECHO_BANKS][:, :], in1=layer2[:, i],
                                      op=ALU.add).then_inc(added, 1)
                    n_second += 1
                elif job[0] == "row_end":
                    i = job[1]
                    if i >= 1:
                        dve.wait_ge(turned_ready, i)
                    dve.wait_ge(tile_jobs_done, done_after[job])
                    dve.tensor_copy(halves[D:P, :], sum_b[i % 2][D:P, :]).then_inc(evac_b, 1)
                elif job[0] == "turn":
                    i = job[1]
                    t = turned[:, :].rearrange("p (c f) -> p c f", c=C)
                    dve.wait_ge(s_res[i % 2], 16 * (i // 2 + 1))
                    if i:
                        dve.wait_ge(h_ready, i)
                    dve.wait_ge(turned_ready, i + 1)
                    step(dve.tensor_tensor(out=r[:, :, :], in0=t[:, :, 0:D],
                                           in1=x_res[:, i % 2].rearrange("p (c d) -> p c d", c=C), op=ALU.add))
                    dve.tensor_tensor(out=r[:, :, :], in0=t[:, :, D:2 * D], in1=r[:, :, :],
                                      op=ALU.add).then_inc(turned_read, 1)
                    dve.wait_ge(turned_read, i + 1)
                    centre(r[:, :, :], C)
                    variance(sq[:, :, :], var[:, 0, 0:C], C)
                    step(inverse_root(rstd[:, 0, 0:C], var[:, 0, 0:C], root[:, 0, 0:C], C, norms))
                    dve.tensor_tensor(out=stat[:, i * C:(i + 1) * C, D:2 * D], in0=r[:, :, :],
                                      in1=over_features(rstd[:, 0, 0:C]), op=ALU.mult).then_inc(h_ready, 1)
                elif job[0] == "final":
                    n = n_final
                    dve.wait_ge(hb_ready, n + 1)
                    dve.wait_ge(product_ready, n + 1)
                    dve.tensor_tensor(out=output_rows(n), in0=product[n % 2][:, :, 0:D], in1=h_bias[n % 2],
                                      op=ALU.add).then_inc(product_read, 1)
                    dve.wait_ge(product_read, n + 1)
                    centre(output_rows(n), 2 * C)
                    if n:
                        pair_inverse_root(n - 1).then_inc(rstd_ready, 1)
                    variance(output_squares(n), var[:, n % 2], 2 * C)
                    n_final += 1
            n = len(finals) - 1
            step(pair_inverse_root(n))
            dve.wait_ge(y_ready, n)
            dve.tensor_tensor(out=output_rows(n), in0=output_rows(n), in1=over_features(rstd[:, n % 2]),
                              op=ALU.mult).then_inc(y_ready, 1)

        @block.tensor
        def _(pe):
            m = 0
            n_second = 0
            n_final = 0
            first_of_row = True
            xu_seen = 0
            h_seen = 0
            first_alone = {}
            for job in jobs:
                if job[0] == "first":
                    first_alone.setdefault(job[1], job)

            def arrived(m):
                slot, use = slot_of[m]
                pe.wait_ge(s_arrived[slot], 16 * (use + 1))
                return slot_ap(slot)

            for at, job in enumerate(jobs):
                kind = job[0]
                if kind in ("fused", "first"):
                    _, i, j = job
                    tile = arrived(m)
                    if i == 0:
                        k = [a <= j < b for a, b in XU_GROUPS].index(True) + 1
                        if k > xu_seen:
                            pe.wait_ge(dropped, k)
                            xu_seen = k
                    if first_of_row and i >= 2:
                        pe.wait_ge(evac_a, max(i - 1, 2 * (i - 1) - 2))
                        pe.wait_ge(evac_b, i - 1)
                    ends = jobs[at + 1] == ("row_end", i)
                    for c in range(C):
                        if kind == "fused":
                            last = pe.matmul(sum_a[i % 2][:, :], stat[:, j * C + c, :], tile[:, c],
                                             start=first_of_row and c == 0, stop=False, skip_group_check=True)
                        elif c % 2 == 0:
                            last = pe.matmul(sum_a[i % 2][0:D, :], stat[:, j * C + c, 0:D], tile[:, c],
                                             start=first_of_row and i < 2 and c == 0, stop=ends and c == 2,
                                             skip_group_check=True)
                        else:
                            last = pe.matmul(sum_b[i % 2][D:P, :], stat[:, j * C + c, 0:D], tile[:, c],
                                             start=("first", i, j) == first_alone[i] and c == 1, stop=ends and c == 3,
                                             skip_group_check=True)
                    last.then_inc(tile_jobs_done, 1)
                    m += 1
                    first_of_row = False
                elif kind == "second":
                    _, i, j = job
                    tile = arrived(m)
                    if j + 1 > h_seen:
                        pe.wait_ge(h_ready, j + 1)
                        h_seen = j + 1
                    if n_second >= ECHO_BANKS:
                        pe.wait_ge(added, n_second - ECHO_BANKS + 1)
                    bank = echo[n_second % ECHO_BANKS]
                    for c in range(C):
                        to = slice(0, D) if c % 2 == 0 else slice(D, P)
                        last = pe.matmul(bank[to, :], stat[:, j * C + c, D:2 * D], tile[:, c],
                                         start=c < 2, stop=c >= 2)
                    last.then_inc(tile_jobs_done, 1)
                    m += 1
                    n_second += 1
                elif kind == "row_end":
                    first_of_row = True
                elif kind == "turn":
                    i = job[1]
                    if i == 0:
                        pe.wait_ge(identity, 1)
                    else:
                        pe.wait_ge(turned_read, i)
                    pe.wait_ge(evac_a, max(i + 1, 2 * (i + 1) - 2 - (i >= 2)))
                    pe.wait_ge(evac_b, i + 1)
                    for c in range(C):
                        last = pe.transpose(turned[:, c * P:(c + 1) * P], halves[:, c * P:(c + 1) * P], ident[:, :])
                    last.then_inc(turned_ready, 1)
                elif kind == "final":
                    i = job[1]
                    if n_final == 0:
                        pe.wait_ge(s_small, 5 * 16)
                    if n_final >= 2:
                        pe.wait_ge(product_read, n_final - 1)
                    else:
                        pe.wait_ge(evac_a, 2 * NB - 2)
                        pe.wait_ge(evac_b, NB)
                    pe.wait_ge(added, complete[i])
                    for c in range(2 * C):
                        last = pe.matmul(product[n_final % 2][:, c], layer2[:, i + c // C, c % C * P:(c % C + 1) * P],
                                         w2[:, :], start=True, stop=True)
                    last.then_inc(product_ready, 1)
                    n_final += 1


_OUT = ((N, D), "float32")


def kernel(x, adj, L0_gnn_u, L1_gnn_weight, L1_gnn_bias):
    import numpy as np
    import concourse.bacc as bacc
    from concourse.bass_utils import run_bass_kernel_spmd

    a = np.asarray(adj).reshape(NB, P, C, NB, P, C).transpose(0, 3, 4, 5, 2, 1)
    arrays = {
        "x": np.ascontiguousarray(x),
        "adj_t": np.ascontiguousarray(a).reshape(NB, NB, P, C, B),
        "u": np.ascontiguousarray(L0_gnn_u),
        "weight": np.ascontiguousarray(L1_gnn_weight),
        "bias": np.ascontiguousarray(L1_gnn_bias),
    }
    nc = bacc.Bacc("TRN2", target_bir_lowering=False, num_devices=1)
    args = [nc.dram_tensor(name, v.shape, F32, kind="ExternalInput").ap() for name, v in arrays.items()]
    out = nc.dram_tensor("out", _OUT[0], F32, kind="ExternalOutput").ap()
    resnorm_graph_layers(nc, *args, out)
    r = run_bass_kernel_spmd(nc, [arrays], core_ids=[0])
    return r.results[0]["out"]
```

```python
import concourse.bass as bass
from concourse import mybir
from contextlib import ExitStack

F32 = mybir.dt.float32
ALU = mybir.AluOpType
ACT = mybir.ActivationFunctionType
AX = mybir.AxisListType

P = 128
N = 8192
D = 64
C = 4
B = C * P
NB = N // B
DROP = 0.1
EPS = 1e-5

SLOTS = 19
LENT_FROM = 4
HOLD = 4
HOLD_MORE = (1, 6, 11)
AGAIN = 3
FILL = 3
ECHO_BANKS = 3
RUN = 8
XU_GROUPS = ((5, 6), (6, 9), (9, 12), (12, 16), (0, 5))
XU_BEFORE = (1, 3, 6, 9)


def held(i, j):
    return i <= j <= i + HOLD + (i in HOLD_MORE) or (i, j) == (1, 0)


def merge(a, b):
    n, m = len(a), len(b)
    keyed = [((k + 0.5) / n, 0, x) for k, x in enumerate(a)] + [((k + 0.5) / m, 1, x) for k, x in enumerate(b)]
    return [x for _, _, x in sorted(keyed, key=lambda t: t[:2])]


def in_runs(a, n):
    return [a[k:k + n] for k in range(0, len(a), n)]


def seconds_of(rows, j):
    jobs = []
    for r in rows:
        if r % 2 == 0 and r + 1 in rows:
            jobs.append(("pair", r, j))
        elif not (r % 2 and r - 1 in rows):
            jobs.append(("second", r, j))
    return jobs


def order_of_work():
    jobs = []
    again = []
    for i in range(NB):
        ready = [("fused", i, j) for j in range(i - 1) if i >= 2]
        late = [("fused", i, i - 1)] if i >= 2 else [("first", i, j) for j in range(i)]
        far = [("first", i, j) for j in range(i + 1, NB) if not held(i, j)]
        near = [("first", i, j) for j in range(NB - 1, i - 1, -1) if held(i, j)]
        if i == 1:
            ready, late = late, []
        if i >= 1:
            filler = []
            for _ in range(FILL):
                filler.append((ready or far).pop(0))
            jobs.append(filler[0])
            jobs.append(("turn", i - 1))
            jobs += filler[1:]
            jobs += seconds_of([r for r in range(NB) if held(r, i - 1)], i - 1)
            again += seconds_of([r for r in range(i - 1) if not held(r, i - 1)], i - 1)
        quota = min(len(again), AGAIN)
        now, again = again[:quota], again[quota:]
        jobs += [job for run in merge(in_runs(ready + late, RUN), in_runs(merge(far, now), RUN)) for job in run]
        jobs += near
        jobs.append(("row_end", i))
    jobs += again[:1]
    jobs.append(("turn", NB - 1))
    jobs += again[1:]
    pending = None
    for i in range(NB - 2, -1, -2):
        jobs.append(("pair", i, NB - 1))
        if pending is not None:
            jobs.append(("final", pending))
        pending = i
    jobs.append(("final", pending))
    return jobs


TILE_JOBS = ("fused", "first", "second", "pair")


def tiles_of(job):
    kind, i, j = job
    return [(i, j), (i + 1, j)] if kind == "pair" else [(i, j)]


def place_tiles(jobs):
    tile_jobs = [job for job in jobs if job[0] in TILE_JOBS]
    needs, on_chip = [], {}
    for m, job in enumerate(tile_jobs):
        for tile in tiles_of(job):
            if tile not in on_chip:
                on_chip[tile] = len(needs)
                needs.append([tile, m, []])
            needs[on_chip[tile]][2].append(m)
            if not (job[0] == "first" and held(*tile)):
                del on_chip[tile]
    row_end = jobs.index(("row_end", 2 * LENT_FROM))
    until = {s: len(tile_jobs) for s in range(SLOTS)}
    until[SLOTS] = sum(job[0] in TILE_JOBS for job in jobs[:row_end])
    free = [(0, s, 0) for s in [*range(SLOTS - 4), SLOTS, *range(SLOTS - 4, SLOTS)]]
    loads, place = [], {}
    for tile, begin, uses in needs:
        free.sort(key=lambda t: t[0])
        found = next(t for t in free if uses[-1] < until[t[1]])
        free.remove(found)
        freed, slot, use = found
        assert freed <= begin, "the order of work needs more slots"
        loads.append((*tile, slot, use, freed))
        free.append((uses[-1] + 1, slot, use + 1))
        for m in uses:
            place[tile_jobs[m], tile] = (slot, use)
    return loads, place


def resnorm_graph_layers(nc: bass.Bass, x, adj_t, u, weight, bias, out):
    jobs = order_of_work()
    loads, place = place_tiles(jobs)

    def evacuated(i):
        return 2 * (i + 1) - min(i + 1, 2)

    done_after, n_tile_jobs = {}, 0
    for job in jobs:
        if job[0] in TILE_JOBS:
            n_tile_jobs += 1
        done_after[job] = n_tile_jobs
    seconds = [job for job in jobs if job[0] in ("second", "pair")]
    finals = [job[1] for job in jobs if job[0] == "final"]
    complete = {i: max(n for n, job in enumerate(seconds) if job[1] in (i, i + 1)) + 1 for i in range(0, NB, 2)}

    x_v = x.rearrange("(b p c) d -> p b (c d)", p=P, c=C)
    u_v = u.rearrange("(b p c) d -> p b (c d)", p=P, c=C)
    out_v = out.rearrange("(b p c) d -> p b (c d)", p=P, c=C)

    ctx = ExitStack()
    with ctx:
        def sb(name, shape):
            return ctx.enter_context(nc.sbuf_tensor(name, shape, F32))

        def sem(name):
            return ctx.enter_context(nc.semaphore(name))

        tiles = sb("tiles", [P, SLOTS, C, B])
        stat = sb("stat", [P, NB * C, 2 * D])
        layer2 = sb("layer2", [P, NB // 2, B])
        x_res = sb("x_res", [P, 2, C * D])
        halves = sb("halves", [P, B])
        work = sb("work", [P, 2, C, D])
        r = work[:, 0]
        sq = work[:, 1]
        sums = sb("sums", [P, 2 * C])
        vsum = sb("vsum", [P, 2 * C])
        var = sb("var", [P, 2, 2 * C])
        root = sb("root", [P, 2, 2 * C])
        newton = sb("newton", [P, 2 * C])
        rstd = sb("rstd", [P, 2, 2 * C])
        h_bias = [x_res[:, :, :].rearrange("p n (c d) -> p (n c) d", d=D),
                  halves[:, :].rearrange("p (c d) -> p c d", d=D)]
        w2 = sb("w2", [P, 2 * D])
        ident = sb("ident", [P, P])
        bias_b = sb("bias_b", [P, D])

        def slot_ap(slot):
            if slot < SLOTS:
                return tiles[:, slot]
            return layer2[:, LENT_FROM:LENT_FROM + C]

        def layer2_block(i):
            return layer2[i % 2 * D:i % 2 * D + D, i // 2]

        staged = SLOTS - 4
        x_stage = tiles[:, staged:staged + 2].rearrange("p s c b -> p (s c b)").rearrange("p (b k) -> p b k", k=C * D)
        u_stage = tiles[:, staged + 2:staged + 4].rearrange("p s c b -> p (s c b)").rearrange("p (b k) -> p b k", k=C * D)

        psum = ctx.enter_context(nc.psum_tensor("psum", [P, 8, B], F32))
        banks = [psum[:, n] for n in range(8)]
        sum_a = banks[0:2]
        sum_b = banks[2:4]
        turned = banks[4]
        echo = banks[5:8]
        product = [psum[:, 2 * n:2 * n + 2].rearrange("p b (c f) -> p (b c) f", c=C) for n in range(2)]

        def over_features(v):
            return v.unsqueeze(2).to_broadcast([*v.shape, D])

        def output_rows(n):
            return layer2[:, finals[n] // 2].rearrange("p (c d) -> p c d", d=D)

        output_squares = work[:, :].rearrange("p n c d -> p (n c) d")

        s_arrived = [sem(f"tile_arrived_{n}") for n in range(SLOTS + 1)]
        s_xu = [sem(f"xu_loaded_{n}") for n in range(len(XU_GROUPS))]
        s_res = [sem(f"x_res_loaded_{n}") for n in range(2)]
        s_small = sem("weight_bias_loaded")
        s_out = sem("out_stored")
        tile_jobs_done = sem("tile_jobs_done")
        dropped = sem("x_dropped")
        zeroed = sem("layer2_zeroed")
        identity = sem("identity_ready")
        evac_a = sem("sum_a_left_psum")
        evac_b = sem("sum_b_left_psum")
        turned_ready = sem("block_turned")
        turned_read = sem("turned_read")
        squared = sem("squared")
        centred = sem("centred")
        var_ready = sem("variance_ready")
        rooted = sem("root_ready")
        rstd_ready = sem("output_scale_ready")
        h_ready = sem("h_ready")
        added = sem("second_added")
        product_ready = sem("product_ready")
        product_read = sem("product_read")
        hb_ready = sem("h_bias_ready")
        y_ready = sem("y_ready")
        pool_step = sem("pool_step")
        dve_step = sem("dve_step")

        row_0 = [job[2] for job in jobs if job[0] in TILE_JOBS][:NB]
        assert row_0 == sorted(row_0, key=lambda j: [a <= j < b for a, b in XU_GROUPS].index(True))

        block = ctx.enter_context(nc.Block())

        @block.sync
        def _(sp):
            def load_xu(g):
                b = slice(*XU_GROUPS[g])
                sp.dma_start(u_stage[:, b], u_v[:, b]).then_inc(s_xu[g], 16)
                sp.dma_start(x_stage[:, b], x_v[:, b]).then_inc(s_xu[g], 16)

            load_xu(0)
            rows_begun = 0
            for n, (i, j, slot, use, freed) in enumerate(loads):
                if n in XU_BEFORE:
                    load_xu(XU_BEFORE.index(n) + 1)
                if n == len(loads) // 2:
                    for at in (0, D):
                        for beside in (0, D):
                            sp.dma_start(w2[at:at + D, beside:beside + D], weight).then_inc(s_small, 16)
                    sp.dma_start(bias_b[:, :], bias.rearrange("(a d) -> a d", a=1).to_broadcast([P, D])).then_inc(s_small, 16)
                if i == rows_begun:
                    if i >= 2:
                        sp.wait_ge(turned_read, i - 1)
                    sp.dma_start(x_res[:, i % 2], x_v[:, i]).then_inc(s_res[i % 2], 16)
                    rows_begun += 1
                if use == 0 and staged <= slot < SLOTS:
                    sp.wait_ge(dropped, len(XU_GROUPS))
                if freed:
                    sp.wait_ge(tile_jobs_done, freed)
                sp.dma_start(slot_ap(slot), adj_t[i, j]).then_inc(s_arrived[slot], 16)
            for n, i in enumerate(finals):
                sp.wait_ge(y_ready, n + 1)
                sp.dma_start(out_v[:, i:i + 2], layer2[:, i // 2].rearrange("p (b k) -> p b k", b=2)).then_inc(s_out, 16)
            sp.wait_ge(s_out, 16 * len(finals))

        @block.gpsimd
        def _(pool):
            pool.memset(layer2[:, 0], 0.0).then_inc(zeroed, 1)
            pool.memset(ident[:, :], 0.0).then_inc(pool_step, 1)
            pool.wait_ge(pool_step, 1)
            pool.affine_select(out=ident[:, :], in_=ident[:, :], compare_op=ALU.not_equal, fill=1.0,
                               base=0, pattern=[[-1, P]], channel_multiplier=1).then_inc(identity, 1)
            pool.wait_ge(s_small, 5 * 16)
            pool.wait_ge(turned_read, NB)
            pool.wait_ge(turned_ready, NB)
            pool.wait_ge(h_ready, NB)

            def scale_pair(n):
                pool.wait_ge(rstd_ready, n + 1)
                pool.tensor_tensor(out=output_rows(n), in0=output_rows(n), in1=over_features(rstd[:, n % 2]),
                                   op=ALU.mult).then_inc(y_ready, 1)

            for n, i in enumerate(finals):
                if n >= 2:
                    pool.wait_ge(product_read, n - 1)
                pool.tensor_tensor(out=h_bias[n % 2], in0=stat[:, i * C:(i + 2) * C, D:2 * D],
                                   in1=bias_b[:, :].unsqueeze(1).to_broadcast([P, 2 * C, D]),
                                   op=ALU.add).then_inc(hb_ready, 1)
                if n >= 2:
                    scale_pair(n - 2)
            scale_pair(len(finals) - 2)

        @block.scalar
        def _(act):
            norms = 0

            def norm(squares, centred_rows, root_ap, var_ap):
                nonlocal norms
                norms += 1
                act.wait_ge(centred, norms)
                act.activation(squares, centred_rows, ACT.Square).then_inc(squared, 1)
                act.wait_ge(var_ready, norms)
                act.activation(root_ap, var_ap, ACT.Sqrt).then_inc(rooted, 1)

            for job in jobs:
                if job[0] == "row_end":
                    i = job[1]
                    if i:
                        act.wait_ge(turned_ready, i)
                    act.wait_ge(tile_jobs_done, done_after[job])
                    act.activation(halves[0:D, :], sum_a[i % 2][0:D, :], ACT.Copy).then_inc(evac_a, 1)
                    if i >= 2:
                        act.activation(layer2_block(i), sum_a[i % 2][D:P, :], ACT.Copy).then_inc(evac_a, 1)
                elif job[0] == "turn":
                    norm(sq[:, :, :], r[:, :, :], root[:, 0, 0:C], var[:, 0, 0:C])
                elif job[0] == "final":
                    i = job[1]
                    n = finals.index(i) % 2
                    norm(output_squares, output_rows(finals.index(i)), root[:, n], var[:, n])

        @block.vector
        def _(dve):
            steps = 0
            norms = 0
            n_second = 0
            n_final = 0

            def step(instruction):
                nonlocal steps
                steps += 1
                instruction.then_inc(dve_step, 1)
                dve.wait_ge(dve_step, steps)

            def centre(rows, n):
                nonlocal norms
                step(dve.tensor_reduce(out=sums[:, 0:n], in_=rows, axis=AX.X, op=ALU.add))
                dve.scalar_tensor_tensor(out=rows, in0=over_features(sums[:, 0:n]),
                                         scalar=-1.0 / D, in1=rows, op0=ALU.mult, op1=ALU.add).then_inc(centred, 1)
                norms += 1

            def variance(squares, var_ap, n):
                dve.wait_ge(squared, norms)
                step(dve.tensor_reduce(out=vsum[:, 0:n], in_=squares, axis=AX.X, op=ALU.add))
                dve.tensor_scalar(var_ap, vsum[:, 0:n], 1.0 / D, EPS, ALU.mult, ALU.add).then_inc(var_ready, 1)

            def inverse_root(rstd_ap, var_ap, root_ap, n, norm):
                dve.wait_ge(rooted, norm)
                step(dve.reciprocal(rstd_ap, root_ap))
                step(dve.tensor_tensor(out=newton[:, 0:n], in0=rstd_ap, in1=rstd_ap, op=ALU.mult))
                step(dve.scalar_tensor_tensor(out=newton[:, 0:n], in0=newton[:, 0:n], scalar=-0.5, in1=var_ap,
                                              op0=ALU.mult, op1=ALU.mult))
                return dve.scalar_tensor_tensor(out=rstd_ap, in0=newton[:, 0:n], scalar=1.5, in1=rstd_ap,
                                                op0=ALU.add, op1=ALU.mult)

            def pair_inverse_root(n):
                if n >= 2:
                    dve.wait_ge(y_ready, n - 1)
                return inverse_root(rstd[:, n % 2], var[:, n % 2], root[:, n % 2], 2 * C, NB + n + 1)

            for n, (begin, end) in enumerate(XU_GROUPS):
                dve.wait_ge(s_xu[n], 32)
                b = slice(begin, end)
                t = slice(begin * C, end * C)
                step(dve.scalar_tensor_tensor(
                    out=stat[:, t, 0:D], in0=u_stage[:, b].rearrange("p b (c d) -> p (b c) d", d=D), scalar=DROP,
                    in1=x_stage[:, b].rearrange("p b (c d) -> p (b c) d", d=D), op0=ALU.is_ge, op1=ALU.mult))
                dve.tensor_scalar(stat[:, t, 0:D], stat[:, t, 0:D], 1.0 / (1.0 - DROP), None, ALU.mult).then_inc(dropped, 1)

            for job in jobs:
                if job[0] in ("second", "pair"):
                    last_row = tiles_of(job)[-1][0]
                    if n_second:
                        dve.wait_ge(added, n_second)
                    else:
                        dve.wait_ge(zeroed, 1)
                    if last_row >= 2:
                        dve.wait_ge(evac_a, evacuated(last_row))
                    dve.wait_ge(tile_jobs_done, done_after[job])
                    bank = echo[n_second % ECHO_BANKS]
                    if job[0] == "pair":
                        to = layer2[:, job[1] // 2]
                        dve.tensor_tensor(out=to, in0=bank[:, :], in1=to, op=ALU.add).then_inc(added, 1)
                    else:
                        to = layer2_block(job[1])
                        step(dve.tensor_tensor(out=to, in0=bank[0:D, :], in1=to, op=ALU.add))
                        dve.tensor_tensor(out=to, in0=bank[D:P, :], in1=to, op=ALU.add).then_inc(added, 1)
                    n_second += 1
                elif job[0] == "row_end":
                    i = job[1]
                    if i >= 1:
                        dve.wait_ge(turned_ready, i)
                    dve.wait_ge(tile_jobs_done, done_after[job])
                    dve.tensor_copy(halves[D:P, :], sum_b[i % 2][D:P, :]).then_inc(evac_b, 1)
                elif job[0] == "turn":
                    i = job[1]
                    t = turned[:, :].rearrange("p (c f) -> p c f", c=C)
                    dve.wait_ge(s_res[i % 2], 16 * (i // 2 + 1))
                    if i:
                        dve.wait_ge(h_ready, i)
                    dve.wait_ge(turned_ready, i + 1)
                    step(dve.tensor_tensor(out=r[:, :, :], in0=t[:, :, 0:D],
                                           in1=x_res[:, i % 2].rearrange("p (c d) -> p c d", c=C), op=ALU.add))
                    dve.tensor_tensor(out=r[:, :, :], in0=t[:, :, D:2 * D], in1=r[:, :, :],
                                      op=ALU.add).then_inc(turned_read, 1)
                    dve.wait_ge(turned_read, i + 1)
                    centre(r[:, :, :], C)
                    variance(sq[:, :, :], var[:, 0, 0:C], C)
                    step(inverse_root(rstd[:, 0, 0:C], var[:, 0, 0:C], root[:, 0, 0:C], C, norms))
                    dve.tensor_tensor(out=stat[:, i * C:(i + 1) * C, D:2 * D], in0=r[:, :, :],
                                      in1=over_features(rstd[:, 0, 0:C]), op=ALU.mult).then_inc(h_ready, 1)
                elif job[0] == "final":
                    n = n_final
                    dve.wait_ge(hb_ready, n + 1)
                    dve.wait_ge(product_ready, n + 1)
                    dve.tensor_tensor(out=output_rows(n), in0=product[n % 2][:, :, 0:D], in1=h_bias[n % 2],
                                      op=ALU.add).then_inc(product_read, 1)
                    dve.wait_ge(product_read, n + 1)
                    centre(output_rows(n), 2 * C)
                    if n:
                        pair_inverse_root(n - 1).then_inc(rstd_ready, 1)
                    variance(output_squares, var[:, n % 2], 2 * C)
                    n_final += 1
            n = len(finals) - 1
            step(pair_inverse_root(n))
            dve.wait_ge(y_ready, n)
            dve.tensor_tensor(out=output_rows(n), in0=output_rows(n), in1=over_features(rstd[:, n % 2]),
                              op=ALU.mult).then_inc(y_ready, 1)

        @block.tensor
        def _(pe):
            n_second = 0
            n_final = 0
            first_of_row = True
            xu_seen = 0
            h_seen = 0
            first_alone = {}
            for job in jobs:
                if job[0] == "first":
                    first_alone.setdefault(job[1], job)

            def arrived(job, tile):
                slot, use = place[job, tile]
                pe.wait_ge(s_arrived[slot], 16 * (use + 1))
                return slot_ap(slot)

            for at, job in enumerate(jobs):
                kind = job[0]
                if kind in ("fused", "first"):
                    _, i, j = job
                    tile = arrived(job, (i, j))
                    if i == 0:
                        k = [a <= j < b for a, b in XU_GROUPS].index(True) + 1
                        if k > xu_seen:
                            pe.wait_ge(dropped, k)
                            xu_seen = k
                    if first_of_row and i >= 2:
                        pe.wait_ge(evac_a, evacuated(i - 2))
                        pe.wait_ge(evac_b, i - 1)
                    ends = jobs[at + 1] == ("row_end", i)
                    for c in range(C):
                        if kind == "fused":
                            last = pe.matmul(sum_a[i % 2][:, :], stat[:, j * C + c, :], tile[:, c],
                                             start=first_of_row and c == 0, stop=False, skip_group_check=True)
                        elif c % 2 == 0:
                            last = pe.matmul(sum_a[i % 2][0:D, :], stat[:, j * C + c, 0:D], tile[:, c],
                                             start=first_of_row and i < 2 and c == 0, stop=ends and c == 2,
                                             skip_group_check=True)
                        else:
                            last = pe.matmul(sum_b[i % 2][D:P, :], stat[:, j * C + c, 0:D], tile[:, c],
                                             start=("first", i, j) == first_alone[i] and c == 1, stop=ends and c == 3,
                                             skip_group_check=True)
                    last.then_inc(tile_jobs_done, 1)
                    first_of_row = False
                elif kind in ("second", "pair"):
                    _, i, j = job
                    moving = [arrived(job, tile) for tile in tiles_of(job)]
                    if j + 1 > h_seen:
                        pe.wait_ge(h_ready, j + 1)
                        h_seen = j + 1
                    if n_second >= ECHO_BANKS:
                        pe.wait_ge(added, n_second - ECHO_BANKS + 1)
                    bank = echo[n_second % ECHO_BANKS]
                    if kind == "pair":
                        for c in range(C):
                            for to, tile in (slice(0, D), moving[0]), (slice(D, P), moving[1]):
                                last = pe.matmul(bank[to, :], stat[:, j * C + c, D:2 * D], tile[:, c],
                                                 start=c == 0, stop=c == C - 1)
                    else:
                        for c in range(C):
                            to = slice(0, D) if c % 2 == 0 else slice(D, P)
                            last = pe.matmul(bank[to, :], stat[:, j * C + c, D:2 * D], moving[0][:, c],
                                             start=c < 2, stop=c >= 2)
                    last.then_inc(tile_jobs_done, 1)
                    n_second += 1
                elif kind == "row_end":
                    first_of_row = True
                elif kind == "turn":
                    i = job[1]
                    if i == 0:
                        pe.wait_ge(identity, 1)
                    else:
                        pe.wait_ge(turned_read, i)
                    pe.wait_ge(evac_a, evacuated(i) - (i >= 2))
                    pe.wait_ge(evac_b, i + 1)
                    for c in range(C):
                        last = pe.transpose(turned[:, c * P:(c + 1) * P], halves[:, c * P:(c + 1) * P], ident[:, :])
                    last.then_inc(turned_ready, 1)
                elif kind == "final":
                    i = job[1]
                    if n_final == 0:
                        pe.wait_ge(s_small, 5 * 16)
                    if n_final >= 2:
                        pe.wait_ge(product_read, n_final - 1)
                    else:
                        pe.wait_ge(evac_a, evacuated(NB - 1))
                        pe.wait_ge(evac_b, NB)
                    pe.wait_ge(added, complete[i])
                    for c in range(C):
                        for to, at in (c, slice(0, D)), (C + c, slice(D, P)):
                            last = pe.matmul(product[n_final % 2][:, to], layer2[at, i // 2, c * P:(c + 1) * P],
                                             w2[at, :], start=True, stop=True)
                    last.then_inc(product_ready, 1)
                    n_final += 1


_OUT = ((N, D), "float32")


def kernel(x, adj, L0_gnn_u, L1_gnn_weight, L1_gnn_bias):
    import numpy as np
    import concourse.bacc as bacc
    from concourse.bass_utils import run_bass_kernel_spmd

    a = np.asarray(adj).reshape(NB, P, C, NB, P, C).transpose(0, 3, 4, 5, 2, 1)
    arrays = {
        "x": np.ascontiguousarray(x),
        "adj_t": np.ascontiguousarray(a).reshape(NB, NB, P, C, B),
        "u": np.ascontiguousarray(L0_gnn_u),
        "weight": np.ascontiguousarray(L1_gnn_weight),
        "bias": np.ascontiguousarray(L1_gnn_bias),
    }
    nc = bacc.Bacc("TRN2", target_bir_lowering=False, num_devices=1)
    args = [nc.dram_tensor(name, v.shape, F32, kind="ExternalInput").ap() for name, v in arrays.items()]
    out = nc.dram_tensor("out", _OUT[0], F32, kind="ExternalOutput").ap()
    resnorm_graph_layers(nc, *args, out)
    r = run_bass_kernel_spmd(nc, [arrays], core_ids=[0])
    return r.results[0]["out"]
```
